# Optimizing a Trainium2 kernel written in Bass

```python
import numpy as np
import jax
import jax.numpy as jnp

def _softmax(x, axis=-1):
    return jax.nn.softmax(x, axis=axis)
def _gelu(x):
    return jax.nn.gelu(x, approximate=True)
def _silu(x):
    return jax.nn.silu(x)
def _sigmoid(x):
    return jax.nn.sigmoid(x)
def _layernorm(x, axis=-1, eps=1e-5):
    m = jnp.mean(x, axis=axis, keepdims=True)
    v = jnp.var(x, axis=axis, keepdims=True)
    return (x - m) / jnp.sqrt(v + eps)
def _scatter_add(tgt, idx, src, axis=0):
    return tgt.at[idx].add(src)
def _segment_sum(src, seg, n):
    return jax.ops.segment_sum(src, seg, n)

kernel_name = 'mk_adj_resnorm_d1_adj_1024_81715f'

def setup_inputs(seed: int = 0):
    np.random.seed(seed)
    _w = jnp.asarray
    def _rec_inputs():
        import jax
        import jax.numpy as jnp
        _gk = jax.random.key(seed)
        x = -0.0002422 + 1 * jax.random.normal(jax.random.fold_in(_gk, 1), (128, 64, 1024), jnp.float32)
        _a = jax.random.bernoulli(jax.random.fold_in(_gk, 2), 0.0625, (128, 64, 64))
        _a = jnp.logical_or(_a, jnp.swapaxes(_a, -1, -2))
        _a = jnp.logical_or(_a, jnp.eye(64, dtype=bool))
        adj = _a.astype(jnp.int32)
        return x, adj
    x, adj = _rec_inputs()
    def _L0_gnn_setup():
        import jax, jax.numpy as jnp
        import numpy as np
        IN_DIM = 1024
        OUT_DIM = 1024
        BATCH = 256
        NUM_OBJS = 100
        key = jax.random.key(seed)
        k1, k2, k3, k4, k5 = jax.random.split(key, 5)
        stdv = 1.0 / np.sqrt(OUT_DIM)
        feature = jax.random.normal(k1, (BATCH, NUM_OBJS, IN_DIM), dtype=jnp.float32)
        graph = jax.random.randint(k2, (BATCH, NUM_OBJS, NUM_OBJS), 0, 2, dtype=jnp.int32)
        weight = jax.random.uniform(k3, (IN_DIM, OUT_DIM), dtype=jnp.float32, minval=-stdv, maxval=stdv)
        wq = jax.random.uniform(k4, (IN_DIM, OUT_DIM), dtype=jnp.float32, minval=-stdv, maxval=stdv)
        wk = jax.random.uniform(k5, (IN_DIM, OUT_DIM), dtype=jnp.float32, minval=-stdv, maxval=stdv)
        return {'feature': feature, 'graph': graph, 'weight': weight, 'wq': wq, 'wk': wk}
    _L0_gnn_all = _L0_gnn_setup()
    _L0_gnn_in = {k: v for k, v in _L0_gnn_all.items() if k in ('weight', 'wq', 'wk', )}
    del _L0_gnn_all

    return {
        "x": x,
        "adj": adj,
        "L0_gnn_weight": _L0_gnn_in["weight"],
        "L0_gnn_wq": _L0_gnn_in["wq"],
        "L0_gnn_wk": _L0_gnn_in["wk"],
    }

def reference(x, adj, L0_gnn_weight, L0_gnn_wq, L0_gnn_wk):
    import jax
    import jax.numpy as jnp
    def _L0_gnn_ref(feature, graph, weight, wq, wk):
        import jax, jax.numpy as jnp
        import numpy as np
        IN_DIM = 1024
        OUT_DIM = 1024
        BATCH = 256
        NUM_OBJS = 100
        output = jnp.einsum('bni,io->bno', feature, weight)
        q = jnp.einsum('bni,io->bno', feature, wq)
        k = jnp.einsum('bni,io->bno', feature, wk)
        alpha = jnp.einsum('bno,bmo->bnm', q, k)
        alpha = jnp.maximum(alpha, 0.0) * (graph != 0).astype(alpha.dtype)
        alpha = jax.nn.softmax(alpha, axis=1)
        return jnp.einsum('bnm,bmo->bno', alpha, output)

    x = _layernorm(x + _L0_gnn_ref(x, adj, L0_gnn_weight, L0_gnn_wq, L0_gnn_wk), axis=-1)
    return x


_drawn_inputs = setup_inputs


def setup_inputs(seed=0):
    import zlib

    import numpy as np

    out = dict(_drawn_inputs(seed))
    spreads = {}
    factors = {}
    for name, (base, spread) in spreads.items():
        noise = np.random.default_rng([zlib.crc32(name.encode()), seed]).standard_normal(out[name].shape)
        drawn = base * np.exp(spread * noise) if base else spread * noise
        out[name] = jnp.asarray(drawn.astype(out[name].dtype))
    for name, factor in factors.items():
        out[name] = (out[name] * factor).astype(out[name].dtype)
    return out
```

```python
import concourse.bass as bass
from concourse import mybir
from contextlib import ExitStack

P = 128
D = 1024
NODES = 64
ROWS = 8192
TILES = 4
GROUPS = ROWS // (TILES * P)
C = D // P
H = 512
EPS = 1e-5
BYTES = 4


def graph_attention_resnorm(nc: bass.Bass, x, x_t, adj_t, w_v, wq_t, wk_t, out):
    f32 = mybir.dt.float32
    f32r = mybir.dt.float32r
    i32 = mybir.dt.int32
    ALU = mybir.AluOpType
    ACT = mybir.ActivationFunctionType
    X = mybir.AxisListType.X

    ctx = ExitStack()
    with ctx:
        top = [(nc.sbuf_base + 31) // 32 * 32]

        def place(name, shape, dtype, at=None):
            size = BYTES
            for n in shape[1:]:
                size *= n
            offset = top[0] if at is None else at
            if at is None:
                top[0] += (size + 31) // 32 * 32
            return nc.alloc_sbuf_tensor_at(name, shape, dtype, offset=offset)

        KIB = 1024
        a0 = top[0]
        raw_w = place("raw_w", [P, C, 2, D], f32)
        m_hi = place("m_hi", [P, C, D], f32r, a0)
        m_lo = place("m_lo", [P, C, D], f32r, a0 + 32 * KIB)
        b0 = top[0]
        wk_hi = place("wk_hi", [P, C, D], f32r)
        wk_lo = place("wk_lo", [P, C, D], f32r)
        wv_hi = place("wv_hi", [P, C, D], f32r, b0)
        wv_lo = place("wv_lo", [P, C, D], f32r, b0 + 32 * KIB)
        c0 = top[0]
        wq_hi = place("wq_hi", [P, 2, C, H], f32r)
        wq_lo = place("wq_lo", [P, 2, C, H], f32r)
        xt_hi = place("xt_hi", [P, C, TILES * P], f32r, c0)
        yt = place("yt", [P, 2, TILES, 2, P], f32r, c0 + 16 * KIB)
        rows_a = place("rows_a", [P, D], f32, c0 + 24 * KIB)
        rows_b = place("rows_b", [P, D], f32, c0 + 28 * KIB)
        xt_lo = place("xt_lo", [P, C, TILES * P], f32r, c0 + 32 * KIB)
        v_hi = place("v_hi", [P, 2, D], f32r, c0 + 48 * KIB)
        v_lo = place("v_lo", [P, 2, D], f32r, c0 + 56 * KIB)
        landing = place("landing", [P, 2, 4, P], f32)
        rows_c = place("rows_c", [P, D], f32)
        attn_hi = place("attn_hi", [P, TILES, P], f32r)
        attn_lo = place("attn_lo", [P, TILES, P], f32r)
        adj_int = place("adj_int", [P, TILES, NODES], i32)
        edge = place("edge", [P, TILES, NODES], f32)
        score = place("score", [P, TILES, NODES], f32)
        peak = place("peak", [P, TILES], f32)
        total = place("total", [P, TILES], f32)
        inv_total = place("inv_total", [P, TILES], f32)
        stats = place("stats", [P, TILES, 2, 6], f32)
        mean_var = place("mean_var", [P, TILES, 2], f32)
        var_eps = place("var_eps", [P, TILES], f32)
        rstd = place("rstd", [P, TILES], f32)
        minus_half = place("minus_half", [P, 1], f32)
        assert top[0] <= nc.sbuf_usable_end, (top[0], nc.sbuf_usable_end)

        ROWS_OF = [0, 1, 0, 2]
        rows = [rows_a, rows_b, rows_c]

        psum = ctx.enter_context(nc.psum_tensor("psum", [P, 8, H], f32))
        proj = [psum[:, 0, :], psum[:, 1, :]]
        score_sum = psum[:, 2:4, :].rearrange("p b (t n) -> p (b t) n", t=2)
        attended = [[psum[:, 4 + 2 * s + h, :] for h in range(2)] for s in range(2)]

        def sem(name):
            return ctx.enter_context(nc.semaphore(name))

        raw_w_loaded = [sem(f"raw_w_loaded{n}") for n in range(2 * C)]
        w_hi_split, w_lo_split = sem("w_hi_split"), sem("w_lo_split")
        m_done, m_hi_ready, m_lo_ready = sem("m_done"), sem("m_hi_ready"), sem("m_lo_ready")
        landed = [sem(f"landed{n}") for n in range(2)]
        land_hi_split, land_lo_split = sem("land_hi_split"), sem("land_lo_split")
        y_done, y_hi_ready, y_lo_ready = sem("y_done"), sem("y_hi_ready"), sem("y_lo_ready")
        scores_done = sem("scores_done")
        xt_front_free = sem("xt_front_free")
        v_done, v_hi_ready, v_lo_ready = sem("v_done"), sem("v_hi_ready"), sem("v_lo_ready")
        attn_zeroed, attn_ready = sem("attn_zeroed"), sem("attn_ready")
        attended_done, residual_added = sem("attended_done"), sem("residual_added")
        adj_loaded, edge_ready = sem("adj_loaded"), sem("edge_ready")
        scores_read = sem("scores_read")
        shifted, exp_done, softmax_step = sem("shifted"), sem("exp_done"), sem("softmax_step")
        stats_done, aggregated, var_ready = sem("stats_done"), sem("aggregated"), sem("var_ready")
        half_set, rstd_ready, normed = sem("half_set"), sem("rstd_ready"), sem("normed")
        rows_loaded = [sem(f"rows_loaded{n}") for n in range(3)]
        rows_stored = [sem(f"rows_stored{n}") for n in range(3)]

        def wait(eng, semaphore, count):
            if not isinstance(count, int) or count > 0:
                eng.wait_ge(semaphore, count)

        X0, W0 = 0, 2 * TILES
        X_PARTS = 2 * TILES

        def x_part(g, t, part):
            if isinstance(g, int) and g == 0:
                return X0 + 2 * t + part
            return g * X_PARTS + (2 * C + 2 * t + part)

        def rows_uses(g, t):
            return g * 2 + t // 2 if ROWS_OF[t] == 0 else g

        def land_count(g, t, part):
            if isinstance(g, int):
                return 16 * (x_part(g, t, part) // 2 + 1)
            return g * (16 * X_PARTS // 2) + 16 * (C + t + 1)

        def m_item(k):
            return (k // 2, k % 2) if k < 8 else (4 + (k - 8) % 4, (k - 8) // 4)

        def every_group(eng, body):
            body(0, True)
            with eng.Fori(1, GROUPS - 1) as g:
                body(g, True)
            body(GROUPS - 1, False)

        block = ctx.enter_context(nc.Block())

        @block.sync
        def _(sp):
            def land(item, source):
                wait(sp, land_lo_split, item - 1)
                sp.dma_start(landing[:, item % 2, :, :].rearrange("p c n -> p (c n)"), source)\
                  .then_inc(landed[item % 2], 16)

            def land_x(g, t):
                for part in range(2):
                    wait(sp, land_lo_split, x_part(g, t, part) - 1)
                    sp.dma_start(landing[:, part, :, :], x_t[g, t, part]).then_inc(landed[part], 16)

            def load_rows(g, t):
                b = ROWS_OF[t]
                wait(sp, rows_stored[b], rows_uses(g, t) * 16)
                sp.dma_start(rows[b][:, :], x[g, t]).then_inc(rows_loaded[b], 16)

            def store_rows(g, t):
                b = ROWS_OF[t]
                wait(sp, normed, g * TILES + (t + 1))
                sp.dma_start(out[g, t], rows[b][:, :]).then_inc(rows_stored[b], 16)

            for d in range(C):
                sp.dma_start(raw_w[:, d, 0, :], wq_t[d]).then_inc(raw_w_loaded[2 * d], 16)
                sp.dma_start(raw_w[:, d, 1, :], wk_t[d]).then_inc(raw_w_loaded[2 * d + 1], 16)
            sp.dma_start(adj_int[:, :, :], adj_t[0]).then_inc(adj_loaded, 16)
            for t in range(TILES):
                land_x(0, t)
            for h in range(2):
                for c in range(C):
                    land(W0 + h * C + c, w_v[h, c])
            sp.wait_ge(m_done, 2 * C)

            def group(g, more):
                if more:
                    land_x(g + 1, 0)
                for t in (0, 1, 3):
                    load_rows(g, t)
                if more:
                    land_x(g + 1, 1)
                    land_x(g + 1, 2)
                store_rows(g, 0)
                load_rows(g, 2)
                if more:
                    land_x(g + 1, 3)
                    sp.wait_ge(edge_ready, g + 1)
                    sp.dma_start(adj_int[:, :, :], adj_t[g + 1]).then_inc(adj_loaded, 16)
                for t in range(1, TILES):
                    store_rows(g, t)

            every_group(sp, group)
            for b in range(3):
                sp.wait_ge(rows_stored[b], 16 * GROUPS * ROWS_OF.count(b))

        @block.tensor
        def _(pe):
            def passes(dst, left, right, first, last):
                nc.tensor.matmul(dst, left[0], right[0], start=first, stop=False)
                nc.tensor.matmul(dst, left[1], right[0], start=False, stop=False)
                return nc.tensor.matmul(dst, left[0], right[1], start=False, stop=last)

            def m_passes(k, d):
                i, h = m_item(k)
                q = slice(i % 4 * P, i % 4 * P + P)
                return passes(psum[:, k % 8, :], (wq_hi[:, i // 4, d, q], wq_lo[:, i // 4, d, q]),
                              (wk_hi[:, d, h * H:(h + 1) * H], wk_lo[:, d, h * H:(h + 1) * H]), d == 0, d == C - 1)

            for d in range(C):
                pe.wait_ge(w_lo_split, 2 * d + 2)
                for k in range(8):
                    last = m_passes(k, d)
                    if d == C - 1:
                        last.then_inc(m_done, 1)
            for k in range(8, 16):
                pe.wait_ge(m_lo_ready, k - 7)
                for d in range(C):
                    last = m_passes(k, d)
                last.then_inc(m_done, 1)

            def y(g, oc):
                if oc < 2:
                    wait(pe, v_lo_ready, g * 8 + (oc - 1))
                else:
                    pe.wait_ge(y_lo_ready, g * 8 + (oc - 1))
                if isinstance(g, int) and g == 0 and oc in (0, 4):
                    pe.wait_ge(m_lo_ready, 12 if oc == 0 else 16)
                for c in range(C):
                    if oc == 0 and c % 4 == 0:
                        pe.wait_ge(land_lo_split, x_part(g, TILES - 1, c // 4) + 1)
                    o = slice(oc * P, oc * P + P)
                    last = passes(proj[oc % 2], (m_hi[:, c, o], m_lo[:, c, o]), (xt_hi[:, c, :], xt_lo[:, c, :]),
                                  c == 0, c == C - 1)
                last.then_inc(y_done, 1)

            def scores(g, oc):
                if oc == 0:
                    wait(pe, scores_read, g * 1)
                pe.wait_ge(y_lo_ready, g * 8 + (oc + 1))
                for t in range(TILES):
                    r = slice(t * P, t * P + P)
                    y_both = yt[:, oc % 2, t, :, :].rearrange("p s n -> p (s n)")
                    nc.tensor.matmul(score_sum[:, t, :], xt_hi[:, oc, r], y_both,
                                     start=(oc == 0 and t % 2 == 0), stop=False, skip_group_check=True)
                    last = nc.tensor.matmul(score_sum[:, t, :], xt_lo[:, oc, r], y_both,
                                            start=False, stop=(oc == C - 1 and t % 2 == 1), skip_group_check=True)
                last.then_inc(scores_done, 1)

            def v(g, t, h):
                if t == 0:
                    pe.wait_ge(y_lo_ready, g * 8 + (7 + h))
                else:
                    pe.wait_ge(v_lo_ready, g * 8 + (2 * t + h - 1))
                if isinstance(g, int) and g == 0 and t == 0:
                    pe.wait_ge(land_lo_split, W0 + C * (h + 1))
                r, o = slice(t * P, t * P + P), slice(h * H, h * H + H)
                for c in range(C):
                    last = passes(proj[h], (xt_hi[:, c, r], xt_lo[:, c, r]), (wv_hi[:, c, o], wv_lo[:, c, o]),
                                  c == 0, c == C - 1)
                    if h == 1 and c == 3:
                        last.then_inc(xt_front_free, 1)
                last.then_inc(v_done, 1)

            def attend(g, t):
                wait(pe, residual_added, g * 8 + (2 * t - 2))
                if t == 0:
                    pe.wait_ge(attn_ready, g + 1)
                for h in range(2):
                    pe.wait_ge(v_lo_ready, g * 8 + (2 * t + h + 1))
                    o = slice(h * H, h * H + H)
                    passes(attended[t % 2][h], (attn_hi[:, t, :], attn_lo[:, t, :]),
                           (v_hi[:, t % 2, o], v_lo[:, t % 2, o]), True, True).then_inc(attended_done, 1)

            def group(g, more):
                y(g, 0)
                for oc in range(1, C):
                    y(g, oc)
                    scores(g, oc - 1)
                v(g, 0, 0)
                scores(g, C - 1)
                v(g, 0, 1)
                for t in range(1, TILES):
                    v(g, t, 0)
                    v(g, t, 1)
                    attend(g, t - 1)
                attend(g, TILES - 1)

            every_group(pe, group)

        @block.scalar
        def _(act):
            def high(dst, src):
                return nc.scalar.activation(dst, src, ACT.Copy)

            def m_high(k):
                i, h = m_item(k)
                act.wait_ge(m_done, k + 1)
                high(m_hi[:, i, h * H:(h + 1) * H], psum[:, k % 8, :]).then_inc(m_hi_ready, 1)

            def x_high(g, t, part):
                act.wait_ge(landed[part], land_count(g, t, part))
                high(xt_hi[:, 4 * part:4 * part + 4, t * P:t * P + P], landing[:, part, :, :])\
                    .then_inc(land_hi_split, 1)

            for d in range(C):
                act.wait_ge(raw_w_loaded[2 * d], 16)
                high(wq_hi[:, :, d, :], raw_w[:, d, 0, :].rearrange("p (h n) -> p h n", h=2)).then_inc(w_hi_split, 1)
                act.wait_ge(raw_w_loaded[2 * d + 1], 16)
                high(wk_hi[:, d, :], raw_w[:, d, 1, :]).then_inc(w_hi_split, 1)
            for k in range(8):
                m_high(k)
            for k in range(8, 16):
                x_high(0, (k - 8) // 2, k % 2)
                m_high(k)

            def wv_high(n):
                item = W0 + n
                act.wait_ge(landed[item % 2], 16 * (item // 2 + 1))
                high(wv_hi[:, n % C, n // C * H:(n // C + 1) * H],
                     landing[:, item % 2, :, :].rearrange("p c n -> p (c n)")).then_inc(land_hi_split, 1)

            def v_high(g, t, h):
                act.wait_ge(v_done, g * 8 + (2 * t + h + 1))
                if h == 0:
                    wait(act, attended_done, g * 8 + (2 * t - 2))
                high(v_hi[:, t % 2, h * H:(h + 1) * H], proj[h]).then_inc(v_hi_ready, 1)

            def group(g, more):
                for oc in range(C):
                    act.wait_ge(y_done, g * 8 + (oc + 1))
                    wait(act, scores_done, g * 8 + (oc - 1))
                    high(yt[:, oc % 2, :, 0, :], proj[oc % 2].rearrange("p (t n) -> p t n", t=TILES))\
                        .then_inc(y_hi_ready, 1)
                    if isinstance(g, int) and g == 0:
                        wv_high(2 * oc)
                        wv_high(2 * oc + 1)
                for t in range(TILES):
                    v_high(g, t, 0)
                    if more:
                        act.wait_ge(xt_front_free, g * TILES + (t + 1))
                        x_high(g + 1, t, 0)
                    v_high(g, t, 1)
                    if more:
                        x_high(g + 1, t, 1)
                    if t == 0:
                        act.wait_ge(shifted, g + 1)
                        nc.scalar.activation(score[:, :, :], score[:, :, :], ACT.Exp).then_inc(exp_done, 1)

            every_group(act, group)

        @block.vector
        def _(dve):
            def low(dst, src, hi):
                return nc.vector.tensor_tensor(dst, src, hi.bitcast(f32), ALU.subtract)

            def m_low(k):
                i, h = m_item(k)
                o = slice(h * H, h * H + H)
                dve.wait_ge(m_hi_ready, k + 1)
                low(m_lo[:, i, o], psum[:, k % 8, :], m_hi[:, i, o]).then_inc(m_lo_ready, 1)

            def x_low(g, t, part):
                dve.wait_ge(land_hi_split, x_part(g, t, part) + 1)
                c, r = slice(4 * part, 4 * part + 4), slice(t * P, t * P + P)
                low(xt_lo[:, c, r], landing[:, part, :, :], xt_hi[:, c, r]).then_inc(land_lo_split, 1)

            for d in range(C):
                dve.wait_ge(w_hi_split, 2 * d + 1)
                low(wq_lo[:, :, d, :], raw_w[:, d, 0, :].rearrange("p (h n) -> p h n", h=2), wq_hi[:, :, d, :])\
                    .then_inc(w_lo_split, 1)
                dve.wait_ge(w_hi_split, 2 * d + 2)
                low(wk_lo[:, d, :], raw_w[:, d, 1, :], wk_hi[:, d, :]).then_inc(w_lo_split, 1)
            for k in range(8):
                m_low(k)
            for k in range(8, 16):
                x_low(0, (k - 8) // 2, k % 2)
                m_low(k)

            def wv_low(n):
                item = W0 + n
                o = slice(n // C * H, (n // C + 1) * H)
                dve.wait_ge(land_hi_split, item + 1)
                low(wv_lo[:, n % C, o], landing[:, item % 2, :, :].rearrange("p c n -> p (c n)"), wv_hi[:, n % C, o])\
                    .then_inc(land_lo_split, 1)

            def v_low(g, t, h):
                o = slice(h * H, h * H + H)
                dve.wait_ge(v_hi_ready, g * 8 + (2 * t + h + 1))
                low(v_lo[:, t % 2, o], proj[h], v_hi[:, t % 2, o]).then_inc(v_lo_ready, 1)

            GRAPHS = [slice(0, NODES), slice(NODES, 2 * NODES)]
            STEPS = 7

            def wide(column):
                return column.unsqueeze(2).to_broadcast([P, TILES, NODES])

            def step(g, n):
                dve.wait_ge(softmax_step, g * STEPS + n)

            def softmax_shift(g):
                dve.wait_ge(adj_loaded, g * 16 + 16)
                nc.vector.tensor_scalar(edge[:, :, :], adj_int[:, :, :], 0.0, None, ALU.not_equal)\
                    .then_inc(edge_ready, 1)
                dve.wait_ge(scores_done, g * 8 + 8)
                for s in GRAPHS:
                    last = nc.vector.tensor_copy(score[s, :, :], score_sum[s, :, P + s.start:P + s.stop])
                last.then_inc(softmax_step, 1)
                step(g, 1)
                for s in GRAPHS:
                    last = nc.vector.tensor_tensor(score[s, :, :], score_sum[s, :, s], score[s, :, :], ALU.add)
                last.then_inc(scores_read, 1)
                dve.wait_ge(scores_read, g + 1)
                dve.wait_ge(edge_ready, g + 1)
                flat = score[:, :, :].rearrange("p t n -> p (t n)")
                nc.vector.scalar_tensor_tensor(flat, flat, 0.0, edge[:, :, :].rearrange("p t n -> p (t n)"),
                                               ALU.max, ALU.mult).then_inc(softmax_step, 1)
                step(g, 2)
                nc.vector.reduce_max(peak[:, :], score[:, :, :], X).then_inc(softmax_step, 1)
                step(g, 3)
                nc.vector.tensor_tensor(score[:, :, :], score[:, :, :], wide(peak[:, :]), ALU.subtract)\
                    .then_inc(shifted, 1)

            def softmax_finish(g):
                dve.wait_ge(exp_done, g + 1)
                nc.vector.reduce_sum(total[:, :], score[:, :, :], X).then_inc(softmax_step, 1)
                step(g, 4)
                nc.vector.reciprocal(inv_total[:, :], total[:, :]).then_inc(softmax_step, 1)
                step(g, 5)
                nc.vector.tensor_tensor(score[:, :, :], score[:, :, :], wide(inv_total[:, :]), ALU.mult)\
                    .then_inc(softmax_step, 1)
                step(g, 6)
                if isinstance(g, int) and g == 0:
                    dve.wait_ge(attn_zeroed, 2)
                wait(dve, attended_done, g * 8)
                for s in GRAPHS:
                    last = nc.vector.tensor_copy(attn_hi[s, :, s], score[s, :, :])
                last.then_inc(softmax_step, 1)
                step(g, 7)
                for s in GRAPHS:
                    last = low(attn_lo[s, :, s], score[s, :, :], attn_hi[s, :, s])
                last.then_inc(attn_ready, 1)

            def residual(g, t):
                b = ROWS_OF[t]
                dve.wait_ge(rows_loaded[b], rows_uses(g, t) * 16 + 16)
                for h in range(2):
                    o = slice(h * H, h * H + H)
                    dve.wait_ge(attended_done, g * 8 + (2 * t + h + 1))
                    nc.vector.tensor_tensor(rows[b][:, o], attended[t % 2][h], rows[b][:, o], ALU.add)\
                        .then_inc(residual_added, 1)
                for h in range(2):
                    dve.wait_ge(residual_added, g * 8 + (2 * t + h + 1))
                    nc.vector.bn_stats(stats[:, t, h, :], rows[b][:, h * H:h * H + H]).then_inc(stats_done, 1)
                dve.wait_ge(attn_zeroed, 2)
                dve.wait_ge(stats_done, g * 8 + (2 * t + 2))
                nc.vector.bn_aggr(mean_var[:, t, :], stats[:, t, :, :].rearrange("p h s -> p (h s)"))\
                    .then_inc(aggregated, 1)
                dve.wait_ge(aggregated, g * TILES + (t + 1))
                nc.vector.tensor_scalar(var_eps[:, t:t + 1], mean_var[:, t, 1:2], EPS, None, ALU.add)\
                    .then_inc(var_ready, 1)

            def normalise(g, t):
                dve.wait_ge(rstd_ready, g * TILES + (t + 1))
                r = rows[ROWS_OF[t]]
                nc.vector.tensor_scalar(r[:, :], r[:, :], mean_var[:, t, 0:1], rstd[:, t:t + 1],
                                        ALU.subtract, ALU.mult).then_inc(normed, 1)

            def group(g, more):
                for oc in range(C):
                    dve.wait_ge(y_hi_ready, g * 8 + (oc + 1))
                    low(yt[:, oc % 2, :, 1, :], proj[oc % 2].rearrange("p (t n) -> p t n", t=TILES),
                        yt[:, oc % 2, :, 0, :]).then_inc(y_lo_ready, 1)
                    if isinstance(g, int) and g == 0:
                        wv_low(2 * oc)
                        wv_low(2 * oc + 1)
                for t in range(TILES):
                    v_low(g, t, 0)
                    if t == 0:
                        softmax_shift(g)
                    if t >= 2:
                        normalise(g, t - 2)
                    if more:
                        x_low(g + 1, t, 0)
                    v_low(g, t, 1)
                    if more:
                        x_low(g + 1, t, 1)
                    if t == 0:
                        softmax_finish(g)
                    else:
                        residual(g, t - 1)
                residual(g, TILES - 1)
                normalise(g, TILES - 2)
                normalise(g, TILES - 1)

            every_group(dve, group)

        @block.gpsimd
        def _(pool):
            for part in (attn_hi, attn_lo):
                nc.gpsimd.memset(part[:, :, :].bitcast(f32), 0.0).then_inc(attn_zeroed, 1)
            nc.gpsimd.memset(minus_half[:, :], -0.5).then_inc(half_set, 1)
            pool.wait_ge(half_set, 1)

            def group(g, more):
                for t in range(TILES):
                    pool.wait_ge(var_ready, g * TILES + (t + 1))
                    nc.gpsimd.tensor_tensor(rstd[:, t:t + 1], var_eps[:, t:t + 1], minus_half[:, :], ALU.pow)\
                        .then_inc(rstd_ready, 1)

            every_group(pool, group)


def kernel(x, adj, L0_gnn_weight, L0_gnn_wq, L0_gnn_wk):
    import numpy as np
    import concourse.bacc as bacc
    from concourse.bass_utils import run_bass_kernel_spmd

    x = np.asarray(x)
    shape = x.shape
    x = np.ascontiguousarray(x).reshape(GROUPS, TILES, P, D)
    x_t = x.reshape(GROUPS, TILES, P, 2, 4, P).transpose(0, 1, 3, 5, 4, 2)
    adj_t = np.asarray(adj).reshape(GROUPS, TILES, 2, NODES, NODES).transpose(0, 2, 4, 1, 3)
    adj_t = adj_t.reshape(GROUPS, P, TILES, NODES)
    w_v = np.asarray(L0_gnn_weight).reshape(C, P, 2, H).transpose(2, 0, 1, 3)
    wq_t = np.asarray(L0_gnn_wq).T.reshape(C, P, D)
    wk_t = np.asarray(L0_gnn_wk).T.reshape(C, P, D)

    nc = bacc.Bacc("TRN2", target_bir_lowering=False, num_devices=1)
    arrays, args = {}, []
    for name, a in (("x", x), ("x_t", x_t), ("adj_t", adj_t), ("w_v", w_v), ("wq_t", wq_t), ("wk_t", wk_t)):
        a = np.ascontiguousarray(a)
        arrays[name] = a
        args.append(nc.dram_tensor(name, a.shape, mybir.dt.from_np(a.dtype), kind="ExternalInput").ap())
    out = nc.dram_tensor("out", (GROUPS, TILES, P, D), mybir.dt.float32, kind="ExternalOutput").ap()
    graph_attention_resnorm(nc, *args, out)
    got = run_bass_kernel_spmd(nc, [arrays], core_ids=[0])
    return got.results[0]["out"].reshape(shape)
```

```python
import concourse.bass as bass
from concourse import mybir
from contextlib import ExitStack

P = 128
D = 1024
NODES = 64
ROWS = 8192
TILES = 4
GROUPS = ROWS // (TILES * P)
C = D // P
H = 512
EPS = 1e-5
BYTES = 4


def graph_attention_resnorm(nc: bass.Bass, x, x_t, adj_t, w_v, wq_t, wk_t, out):
    f32 = mybir.dt.float32
    f32r = mybir.dt.float32r
    i32 = mybir.dt.int32
    ALU = mybir.AluOpType
    ACT = mybir.ActivationFunctionType
    X = mybir.AxisListType.X

    ctx = ExitStack()
    with ctx:
        top = [(nc.sbuf_base + 31) // 32 * 32]

        def place(name, shape, dtype, at=None):
            size = BYTES
            for n in shape[1:]:
                size *= n
            offset = top[0] if at is None else at
            if at is None:
                top[0] += (size + 31) // 32 * 32
            return nc.alloc_sbuf_tensor_at(name, shape, dtype, offset=offset)

        KIB = 1024
        a0 = top[0]
        raw_wq = place("raw_wq", [P, 2, C, H], f32)
        raw_wk = place("raw_wk", [P, C, D], f32)
        m_hi = place("m_hi", [P, C, D], f32r, a0)
        m_lo = place("m_lo", [P, C, D], f32r, a0 + 32 * KIB)
        b0 = top[0]
        wk_hi = place("wk_hi", [P, C, D], f32r)
        wk_lo = place("wk_lo", [P, C, D], f32r)
        wv_hi = place("wv_hi", [P, C, D], f32r, b0)
        wv_lo = place("wv_lo", [P, C, D], f32r, b0 + 32 * KIB)
        c0 = top[0]
        wq_hi = place("wq_hi", [P, 2, C, H], f32r)
        wq_lo = place("wq_lo", [P, 2, C, H], f32r)
        xt_hi = place("xt_hi", [P, C, TILES * P], f32r, c0)
        yt = place("yt", [P, 2, TILES, 2, P], f32r, c0 + 16 * KIB)
        rows_a = place("rows_a", [P, D], f32, c0 + 24 * KIB)
        rows_b = place("rows_b", [P, D], f32, c0 + 28 * KIB)
        xt_lo = place("xt_lo", [P, C, TILES * P], f32r, c0 + 32 * KIB)
        v_split = place("v_split", [P, 2, 2, D], f32r, c0 + 48 * KIB)
        landing = place("landing", [P, 2, 4, P], f32)
        rows_c = place("rows_c", [P, D], f32)
        attn = place("attn", [P, TILES, 2, 2, NODES], f32r)
        gathered = place("gathered", [P, 2, D], f32)
        adj_int = place("adj_int", [P, TILES, NODES], i32)
        edge = place("edge", [P, TILES, NODES], f32)
        score = place("score", [P, TILES, NODES], f32)
        peak = place("peak", [P, TILES], f32)
        total = place("total", [P, TILES], f32)
        inv_total = place("inv_total", [P, TILES], f32)
        stats = place("stats", [P, TILES, 2, 6], f32)
        mean_var = place("mean_var", [P, TILES, 2], f32)
        var_eps = place("var_eps", [P, TILES], f32)
        rstd = place("rstd", [P, TILES], f32)
        minus_half = place("minus_half", [P, 1], f32)
        assert top[0] <= nc.sbuf_usable_end, (top[0], nc.sbuf_usable_end)

        ROWS_OF = [0, 1, 0, 2]
        rows = [rows_a, rows_b, rows_c]

        psum = ctx.enter_context(nc.psum_tensor("psum", [P, 8, H], f32))
        proj = [psum[:, 0, :], psum[:, 1, :]]
        score_sum = psum[:, 2:4, :].rearrange("p b (t n) -> p (b t) n", t=2)
        attended = [psum[:, 4 + 2 * b:6 + 2 * b, :].rearrange("p h n -> p (h n)") for b in range(2)]
        GRAPHS = [slice(0, NODES), slice(NODES, 2 * NODES)]

        def sem(name):
            return ctx.enter_context(nc.semaphore(name))

        raw_w_loaded = [sem(f"raw_w_loaded{n}") for n in range(4 * C)]
        w_hi_split, w_lo_split = sem("w_hi_split"), sem("w_lo_split")
        m_done, m_hi_ready, m_lo_ready = sem("m_done"), sem("m_hi_ready"), sem("m_lo_ready")
        landed = [sem(f"landed{n}") for n in range(2)]
        land_hi_split, land_lo_split = sem("land_hi_split"), sem("land_lo_split")
        y_done, y_hi_ready, y_lo_ready = sem("y_done"), sem("y_hi_ready"), sem("y_lo_ready")
        scores_done = sem("scores_done")
        xt_front_free = sem("xt_front_free")
        v_done, v_hi_ready, v_lo_ready = sem("v_done"), sem("v_hi_ready"), sem("v_lo_ready")
        attn_hi_ready, attn_ready = sem("attn_hi_ready"), sem("attn_ready")
        attended_done, gathered_ready = sem("attended_done"), sem("gathered_ready")
        residual_added = sem("residual_added")
        adj_loaded, edge_ready = sem("adj_loaded"), sem("edge_ready")
        scores_read = sem("scores_read")
        shifted, exp_done, softmax_step = sem("shifted"), sem("exp_done"), sem("softmax_step")
        stats_done, aggregated, var_ready = sem("stats_done"), sem("aggregated"), sem("var_ready")
        half_set, rstd_ready, normed = sem("half_set"), sem("rstd_ready"), sem("normed")
        rows_loaded = [sem(f"rows_loaded{n}") for n in range(3)]
        rows_stored = [sem(f"rows_stored{n}") for n in range(3)]

        def wait(eng, semaphore, count):
            if not isinstance(count, int) or count > 0:
                eng.wait_ge(semaphore, count)

        X0, W0 = 0, 2 * TILES
        X_PARTS = 2 * TILES

        def x_part(g, t, part):
            if isinstance(g, int) and g == 0:
                return X0 + 2 * t + part
            return g * X_PARTS + (2 * C + 2 * t + part)

        def rows_uses(g, t):
            return g * 2 + t // 2 if ROWS_OF[t] == 0 else g

        def land_count(g, t, part):
            if isinstance(g, int):
                return 16 * (x_part(g, t, part) // 2 + 1)
            return g * (16 * X_PARTS // 2) + 16 * (C + t + 1)

        def m_item(k):
            return 4 * (k // 8) + k % 4, k % 8 // 4

        W_PARTS = []
        for d in range(C):
            W_PARTS.append((raw_wq[:, 0, d, :], wq_hi[:, 0, d, :], wq_lo[:, 0, d, :], wq_t[0, d]))
            for h in range(2):
                o = slice(h * H, h * H + H)
                W_PARTS.append((raw_wk[:, d, o], wk_hi[:, d, o], wk_lo[:, d, o], wk_t[d, :, o]))
        for d in range(C):
            W_PARTS.append((raw_wq[:, 1, d, :], wq_hi[:, 1, d, :], wq_lo[:, 1, d, :], wq_t[1, d]))

        def every_group(eng, body):
            body(0, False, True)
            with eng.Fori(1, GROUPS - 1) as g:
                body(g, True, True)
            body(GROUPS - 1, True, False)

        block = ctx.enter_context(nc.Block())

        @block.sync
        def _(sp):
            def land(item, source):
                wait(sp, land_lo_split, item - 1)
                sp.dma_start(landing[:, item % 2, :, :].rearrange("p c n -> p (c n)"), source)\
                  .then_inc(landed[item % 2], 16)

            def land_x(g, t):
                for part in range(2):
                    wait(sp, land_lo_split, x_part(g, t, part) - 1)
                    sp.dma_start(landing[:, part, :, :], x_t[g, t, part]).then_inc(landed[part], 16)

            def load_rows(g, t):
                b = ROWS_OF[t]
                wait(sp, rows_stored[b], rows_uses(g, t) * 16)
                sp.dma_start(rows[b][:, :], x[g, t]).then_inc(rows_loaded[b], 16)

            def store_rows(g, t):
                b = ROWS_OF[t]
                wait(sp, normed, g * TILES + (t + 1))
                sp.dma_start(out[g, t], rows[b][:, :]).then_inc(rows_stored[b], 16)

            for n, (raw, _, _, source) in enumerate(W_PARTS):
                sp.dma_start(raw, source).then_inc(raw_w_loaded[n], 16)
            sp.dma_start(adj_int[:, :, :], adj_t[0]).then_inc(adj_loaded, 16)
            for t in range(TILES):
                land_x(0, t)
            for h in range(2):
                for c in range(C):
                    land(W0 + h * C + c, w_v[h, c])
            sp.wait_ge(m_done, 2 * C)

            def group(g, before, more):
                if more:
                    land_x(g + 1, 0)
                if before:
                    store_rows(g - 1, 2)
                    store_rows(g - 1, 3)
                for t in (0, 1, 3):
                    load_rows(g, t)
                if more:
                    land_x(g + 1, 1)
                    land_x(g + 1, 2)
                store_rows(g, 0)
                load_rows(g, 2)
                if more:
                    land_x(g + 1, 3)
                    sp.wait_ge(edge_ready, g + 1)
                    sp.dma_start(adj_int[:, :, :], adj_t[g + 1]).then_inc(adj_loaded, 16)
                store_rows(g, 1)

            every_group(sp, group)
            store_rows(GROUPS - 1, 2)
            store_rows(GROUPS - 1, 3)
            for b in range(3):
                sp.wait_ge(rows_stored[b], 16 * GROUPS * ROWS_OF.count(b))

        @block.tensor
        def _(pe):
            def passes(dst, left, right, first, last):
                nc.tensor.matmul(dst, left[0], right[0], start=first, stop=False)
                nc.tensor.matmul(dst, left[0], right[1], start=False, stop=False)
                return nc.tensor.matmul(dst, left[1], right[0], start=False, stop=last)

            def m_passes(k, d):
                i, h = m_item(k)
                q = slice(i % 4 * P, i % 4 * P + P)
                return passes(psum[:, k % 8, :], (wq_hi[:, i // 4, d, q], wq_lo[:, i // 4, d, q]),
                              (wk_hi[:, d, h * H:(h + 1) * H], wk_lo[:, d, h * H:(h + 1) * H]), d == 0, d == C - 1)

            for d in range(C):
                for k in range(8):
                    if k % 4 == 0:
                        pe.wait_ge(w_lo_split, 3 * d + 2 + k // 4)
                    last = m_passes(k, d)
                    if d == C - 1:
                        last.then_inc(m_done, 1)
            for k in range(8, 16):
                pe.wait_ge(m_lo_ready, k - 7)
                if k == 8:
                    pe.wait_ge(w_lo_split, 4 * C)
                for d in range(C):
                    last = m_passes(k, d)
                last.then_inc(m_done, 1)

            def y(g, oc):
                if oc < 2:
                    wait(pe, v_lo_ready, g * 8 + (oc - 1))
                else:
                    pe.wait_ge(y_lo_ready, g * 8 + (oc - 1))
                if isinstance(g, int) and g == 0 and oc in (0, 4):
                    pe.wait_ge(m_lo_ready, 12 if oc == 0 else 16)
                for c in range(C):
                    if oc == 0 and c % 4 == 0:
                        pe.wait_ge(land_lo_split, x_part(g, TILES - 1, c // 4) + 1)
                    o = slice(oc * P, oc * P + P)
                    last = passes(proj[oc % 2], (m_hi[:, c, o], m_lo[:, c, o]), (xt_hi[:, c, :], xt_lo[:, c, :]),
                                  c == 0, c == C - 1)
                last.then_inc(y_done, 1)

            def scores(g, oc):
                if oc == 0:
                    wait(pe, scores_read, g * 1)
                pe.wait_ge(y_lo_ready, g * 8 + (oc + 1))
                for t in range(TILES):
                    r = slice(t * P, t * P + P)
                    y_both = yt[:, oc % 2, t, :, :].rearrange("p s n -> p (s n)")
                    nc.tensor.matmul(score_sum[:, t, :], xt_hi[:, oc, r], y_both,
                                     start=(oc == 0 and t % 2 == 0), stop=False, skip_group_check=True)
                    last = nc.tensor.matmul(score_sum[:, t, :], xt_lo[:, oc, r], y_both,
                                            start=False, stop=(oc == C - 1 and t % 2 == 1), skip_group_check=True)
                last.then_inc(scores_done, 1)

            def v(g, t, h):
                if t == 0:
                    pe.wait_ge(y_lo_ready, g * 8 + (7 + h))
                else:
                    pe.wait_ge(v_lo_ready, g * 8 + (2 * t + h - 1))
                if isinstance(g, int) and g == 0 and t == 0:
                    pe.wait_ge(land_lo_split, W0 + C * (h + 1))
                r, o = slice(t * P, t * P + P), slice(h * H, h * H + H)
                for c in range(C):
                    last = passes(proj[h], (xt_hi[:, c, r], xt_lo[:, c, r]), (wv_hi[:, c, o], wv_lo[:, c, o]),
                                  c == 0, c == C - 1)
                    if h == 1 and c == 3:
                        last.then_inc(xt_front_free, 1)
                last.then_inc(v_done, 1)

            def attend(g, t):
                wait(pe, gathered_ready, g * 16 + 4 * t)
                if t == 0:
                    pe.wait_ge(attn_ready, g + 1)
                for h in range(2):
                    o = slice(h * H, h * H + H)
                    pe.wait_ge(v_lo_ready, g * 8 + (2 * t + h + 1))
                    for b in range(2):
                        last = nc.tensor.matmul(attended[b][:, o], attn[:, t, b, :, :].rearrange("p s n -> p (s n)"),
                                                v_split[:, t % 2, b, o], start=True, stop=True)
                    last.then_inc(attended_done, 1)

            def group(g, before, more):
                y(g, 0)
                y(g, 1)
                if before:
                    attend(g - 1, TILES - 1)
                scores(g, 0)
                for oc in range(2, C):
                    y(g, oc)
                    scores(g, oc - 1)
                v(g, 0, 0)
                scores(g, C - 1)
                v(g, 0, 1)
                for t in range(1, TILES):
                    v(g, t, 0)
                    if not more and t == TILES - 1:
                        attend(g, t - 1)
                        v(g, t, 1)
                    else:
                        v(g, t, 1)
                        attend(g, t - 1)

            every_group(pe, group)
            attend(GROUPS - 1, TILES - 1)

        @block.scalar
        def _(act):
            def high(dst, src):
                return nc.scalar.activation(dst, src, ACT.Copy)

            def m_high(k):
                i, h = m_item(k)
                act.wait_ge(m_done, k + 1)
                high(m_hi[:, i, h * H:(h + 1) * H], psum[:, k % 8, :]).then_inc(m_hi_ready, 1)

            def x_high(g, t, part):
                act.wait_ge(landed[part], land_count(g, t, part))
                high(xt_hi[:, 4 * part:4 * part + 4, t * P:t * P + P], landing[:, part, :, :])\
                    .then_inc(land_hi_split, 1)

            for n, (raw, w_hi, _, _) in enumerate(W_PARTS):
                act.wait_ge(raw_w_loaded[n], 16)
                high(w_hi, raw).then_inc(w_hi_split, 1)
            for k in range(8):
                m_high(k)
            for k in range(8, 16):
                x_high(0, (k - 8) // 2, k % 2)
                m_high(k)

            def wv_high(n):
                item = W0 + n
                act.wait_ge(landed[item % 2], 16 * (item // 2 + 1))
                high(wv_hi[:, n % C, n // C * H:(n // C + 1) * H],
                     landing[:, item % 2, :, :].rearrange("p c n -> p (c n)")).then_inc(land_hi_split, 1)

            def v_high(g, t, h):
                act.wait_ge(v_done, g * 8 + (2 * t + h + 1))
                if h == 0:
                    wait(act, attended_done, g * 8 + (2 * t - 2))
                for b, rows_b in enumerate(GRAPHS):
                    high(v_split[rows_b, t % 2, b, h * H:(h + 1) * H], proj[h][rows_b, :]).then_inc(v_hi_ready, 1)

            def gather(g, t):
                for h in range(2):
                    act.wait_ge(attended_done, g * 8 + (2 * t + h + 1))
                    o = slice(h * H, h * H + H)
                    for part in range(2):
                        wait(act, residual_added, g * 16 + (4 * t + 2 * h + part - 3))
                        for b in range(2):
                            last = nc.scalar.activation(gathered[GRAPHS[b], part, o], attended[b][GRAPHS[part], o],
                                                        ACT.Copy)
                        last.then_inc(gathered_ready, 1)

            def group(g, before, more):
                for oc in range(C):
                    act.wait_ge(y_done, g * 8 + (oc + 1))
                    wait(act, scores_done, g * 8 + (oc - 1))
                    high(yt[:, oc % 2, :, 0, :], proj[oc % 2].rearrange("p (t n) -> p t n", t=TILES))\
                        .then_inc(y_hi_ready, 1)
                    if not before:
                        wv_high(2 * oc)
                        wv_high(2 * oc + 1)
                    elif oc == 1:
                        gather(g - 1, TILES - 1)
                for t in range(TILES):
                    v_high(g, t, 0)
                    if more:
                        act.wait_ge(xt_front_free, g * TILES + (t + 1))
                        x_high(g + 1, t, 0)
                        act.wait_ge(v_done, g * 8 + (2 * t + 2))
                        x_high(g + 1, t, 1)
                    if not more and t == TILES - 1:
                        gather(g, t - 1)
                    v_high(g, t, 1)
                    if t == 0:
                        act.wait_ge(shifted, g + 1)
                        nc.scalar.activation(score[:, :, :], score[:, :, :], ACT.Exp).then_inc(exp_done, 1)
                    elif more or t < TILES - 1:
                        gather(g, t - 1)

            every_group(act, group)
            gather(GROUPS - 1, TILES - 1)

        @block.vector
        def _(dve):
            def low(dst, src, hi):
                return nc.vector.tensor_tensor(dst, src, hi.bitcast(f32), ALU.subtract)

            def m_low(k):
                i, h = m_item(k)
                o = slice(h * H, h * H + H)
                dve.wait_ge(m_hi_ready, k + 1)
                low(m_lo[:, i, o], psum[:, k % 8, :], m_hi[:, i, o]).then_inc(m_lo_ready, 1)

            def x_low(g, t, part):
                dve.wait_ge(land_hi_split, x_part(g, t, part) + 1)
                c, r = slice(4 * part, 4 * part + 4), slice(t * P, t * P + P)
                low(xt_lo[:, c, r], landing[:, part, :, :], xt_hi[:, c, r]).then_inc(land_lo_split, 1)

            for n, (raw, w_hi, w_lo, _) in enumerate(W_PARTS):
                dve.wait_ge(w_hi_split, n + 1)
                low(w_lo, raw, w_hi).then_inc(w_lo_split, 1)
            for k in range(8):
                m_low(k)
            for k in range(8, 16):
                x_low(0, (k - 8) // 2, k % 2)
                m_low(k)

            def wv_low(n):
                item = W0 + n
                o = slice(n // C * H, (n // C + 1) * H)
                dve.wait_ge(land_hi_split, item + 1)
                low(wv_lo[:, n % C, o], landing[:, item % 2, :, :].rearrange("p c n -> p (c n)"), wv_hi[:, n % C, o])\
                    .then_inc(land_lo_split, 1)

            def v_low(g, t, h):
                o = slice(h * H, h * H + H)
                for b in range(2):
                    dve.wait_ge(v_hi_ready, g * 16 + (4 * t + 2 * h + b + 1))
                    last = low(v_split[GRAPHS[1 - b], t % 2, b, o], proj[h][GRAPHS[b], :],
                               v_split[GRAPHS[b], t % 2, b, o])
                last.then_inc(v_lo_ready, 1)

            STEPS = 6

            def wide(column):
                return column.unsqueeze(2).to_broadcast([P, TILES, NODES])

            def step(g, n):
                dve.wait_ge(softmax_step, g * STEPS + n)

            def softmax_shift(g):
                dve.wait_ge(adj_loaded, g * 16 + 16)
                nc.vector.tensor_scalar(edge[:, :, :], adj_int[:, :, :], 0.0, None, ALU.not_equal)\
                    .then_inc(edge_ready, 1)
                dve.wait_ge(scores_done, g * 8 + 8)
                for s in GRAPHS:
                    last = nc.vector.tensor_copy(score[s, :, :], score_sum[s, :, P + s.start:P + s.stop])
                last.then_inc(softmax_step, 1)
                step(g, 1)
                for s in GRAPHS:
                    last = nc.vector.tensor_tensor(score[s, :, :], score_sum[s, :, s], score[s, :, :], ALU.add)
                last.then_inc(scores_read, 1)
                dve.wait_ge(scores_read, g + 1)
                dve.wait_ge(edge_ready, g + 1)
                flat = score[:, :, :].rearrange("p t n -> p (t n)")
                nc.vector.scalar_tensor_tensor(flat, flat, 0.0, edge[:, :, :].rearrange("p t n -> p (t n)"),
                                               ALU.max, ALU.mult).then_inc(softmax_step, 1)
                step(g, 2)
                nc.vector.reduce_max(peak[:, :], score[:, :, :], X).then_inc(softmax_step, 1)
                step(g, 3)
                nc.vector.tensor_tensor(score[:, :, :], score[:, :, :], wide(peak[:, :]), ALU.subtract)\
                    .then_inc(shifted, 1)

            def softmax_finish(g):
                dve.wait_ge(exp_done, g + 1)
                nc.vector.reduce_sum(total[:, :], score[:, :, :], X).then_inc(softmax_step, 1)
                step(g, 4)
                nc.vector.reciprocal(inv_total[:, :], total[:, :]).then_inc(softmax_step, 1)
                step(g, 5)
                nc.vector.tensor_tensor(score[:, :, :], score[:, :, :], wide(inv_total[:, :]), ALU.mult)\
                    .then_inc(softmax_step, 1)
                step(g, 6)
                wait(dve, attended_done, g * 8)
                for b in range(2):
                    for half in (b, 1 - b):
                        last = nc.vector.tensor_copy(attn[GRAPHS[half], :, b, 0, :], score[GRAPHS[b], :, :])
                last.then_inc(attn_hi_ready, 1)
                dve.wait_ge(attn_hi_ready, g + 1)
                for b in range(2):
                    for half in range(2):
                        last = low(attn[GRAPHS[half], :, b, 1, :], score[GRAPHS[b], :, :], attn[GRAPHS[b], :, b, 0, :])
                last.then_inc(attn_ready, 1)

            def residual(g, t):
                b = ROWS_OF[t]
                dve.wait_ge(rows_loaded[b], rows_uses(g, t) * 16 + 16)
                for h in range(2):
                    o = slice(h * H, h * H + H)
                    for part in range(2):
                        n = 4 * t + 2 * h + part + 1
                        dve.wait_ge(gathered_ready, g * 16 + n)
                        if part:
                            dve.wait_ge(residual_added, g * 16 + (n - 1))
                        nc.vector.tensor_tensor(rows[b][:, o], gathered[:, part, o], rows[b][:, o], ALU.add)\
                            .then_inc(residual_added, 1)
                    dve.wait_ge(residual_added, g * 16 + n)
                    nc.vector.bn_stats(stats[:, t, h, :], rows[b][:, o]).then_inc(stats_done, 2)
                dve.wait_ge(w_lo_split, 4 * C)
                dve.wait_ge(stats_done, g * 16 + n)
                nc.vector.bn_aggr(mean_var[:, t, :], stats[:, t, :, :].rearrange("p h s -> p (h s)"))\
                    .then_inc(aggregated, 1)
                dve.wait_ge(aggregated, g * TILES + (t + 1))
                nc.vector.tensor_scalar(var_eps[:, t:t + 1], mean_var[:, t, 1:2], EPS, None, ALU.add)\
                    .then_inc(var_ready, 1)

            def normalise(g, t):
                dve.wait_ge(rstd_ready, g * TILES + (t + 1))
                r = rows[ROWS_OF[t]]
                nc.vector.tensor_scalar(r[:, :], r[:, :], mean_var[:, t, 0:1], rstd[:, t:t + 1],
                                        ALU.subtract, ALU.mult).then_inc(normed, 1)

            def group(g, before, more):
                for oc in range(C):
                    dve.wait_ge(y_hi_ready, g * 8 + (oc + 1))
                    low(yt[:, oc % 2, :, 1, :], proj[oc % 2].rearrange("p (t n) -> p t n", t=TILES),
                        yt[:, oc % 2, :, 0, :]).then_inc(y_lo_ready, 1)
                    if not before:
                        wv_low(2 * oc)
                        wv_low(2 * oc + 1)
                    elif oc == 0:
                        normalise(g - 1, 2)
                    elif oc == 1:
                        residual(g - 1, 3)
                    elif oc == 2:
                        normalise(g - 1, 3)
                for t in range(TILES):
                    v_low(g, t, 0)
                    if t == 0:
                        softmax_shift(g)
                    if t >= 2:
                        normalise(g, t - 2)
                    if more:
                        x_low(g + 1, t, 0)
                        x_low(g + 1, t, 1)
                    early = not more and t == TILES - 1
                    if early:
                        residual(g, t - 1)
                    v_low(g, t, 1)
                    if t == 0:
                        softmax_finish(g)
                    elif not early:
                        residual(g, t - 1)

            every_group(dve, group)
            normalise(GROUPS - 1, 2)
            residual(GROUPS - 1, 3)
            normalise(GROUPS - 1, 3)

        @block.gpsimd
        def _(pool):
            nc.gpsimd.memset(minus_half[:, :], -0.5).then_inc(half_set, 1)
            pool.wait_ge(half_set, 1)

            def group(g, before, more):
                for t in range(TILES):
                    pool.wait_ge(var_ready, g * TILES + (t + 1))
                    nc.gpsimd.tensor_tensor(rstd[:, t:t + 1], var_eps[:, t:t + 1], minus_half[:, :], ALU.pow)\
                        .then_inc(rstd_ready, 1)

            every_group(pool, group)


def kernel(x, adj, L0_gnn_weight, L0_gnn_wq, L0_gnn_wk):
    import numpy as np
    import concourse.bacc as bacc
    from concourse.bass_utils import run_bass_kernel_spmd

    x = np.asarray(x)
    shape = x.shape
    x = np.ascontiguousarray(x).reshape(GROUPS, TILES, P, D)
    x_t = x.reshape(GROUPS, TILES, P, 2, 4, P).transpose(0, 1, 3, 5, 4, 2)
    adj_t = np.asarray(adj).reshape(GROUPS, TILES, 2, NODES, NODES).transpose(0, 2, 4, 1, 3)
    adj_t = adj_t.reshape(GROUPS, P, TILES, NODES)
    w_v = np.asarray(L0_gnn_weight).reshape(C, P, 2, H).transpose(2, 0, 1, 3)
    wq_t = np.asarray(L0_gnn_wq).T.reshape(C, P, 2, H).transpose(2, 0, 1, 3)
    wk_t = np.asarray(L0_gnn_wk).T.reshape(C, P, D)

    nc = bacc.Bacc("TRN2", target_bir_lowering=False, num_devices=1,
                   dynamic_dma_scratch_size=4096)
    arrays, args = {}, []
    for name, a in (("x", x), ("x_t", x_t), ("adj_t", adj_t), ("w_v", w_v), ("wq_t", wq_t), ("wk_t", wk_t)):
        a = np.ascontiguousarray(a)
        arrays[name] = a
        args.append(nc.dram_tensor(name, a.shape, mybir.dt.from_np(a.dtype), kind="ExternalInput").ap())
    out = nc.dram_tensor("out", (GROUPS, TILES, P, D), mybir.dt.float32, kind="ExternalOutput").ap()
    graph_attention_resnorm(nc, *args, out)
    got = run_bass_kernel_spmd(nc, [arrays], core_ids=[0])
    return got.results[0]["out"].reshape(shape)
```
